# Optimizing a Trainium2 kernel written in Bass

```python
import numpy as np
import jax
import jax.numpy as jnp

def _softmax(x, axis=-1):
    return jax.nn.softmax(x, axis=axis)

def _gelu(x):
    return jax.nn.gelu(x, approximate=True)

def _silu(x):
    return jax.nn.silu(x)

def _sigmoid(x):
    return jax.nn.sigmoid(x)

def _layernorm(x, axis=-1, eps=1e-05):
    m = jnp.mean(x, axis=axis, keepdims=True)
    v = jnp.var(x, axis=axis, keepdims=True)
    return (x - m) / jnp.sqrt(v + eps)

def _scatter_add(tgt, idx, src, axis=0):
    return tgt.at[idx].add(src)

def _segment_sum(src, seg, n):
    return jax.ops.segment_sum(src, seg, n)
kernel_name = 'mk_flamingo_gated_d1_seqx_r4_0b10ec'

def setup_inputs(seed: int=0):
    np.random.seed(seed)
    _w = jnp.asarray

    def _rec_inputs():
        import jax
        import jax.numpy as jnp
        _rk = jax.random.key(seed)
        x = -0.000125 + 0.9999 * jax.random.normal(jax.random.fold_in(_rk, 1), (32, 100, 512), jnp.float32)
        _lenS = 100 - jax.random.randint(jax.random.fold_in(_rk, 7), (32,), 0, max(1, 100 // 4) + 1, jnp.int32)
        _lenS2 = 361 - jax.random.randint(jax.random.fold_in(_rk, 8), (32,), 0, max(1, 361 // 4) + 1, jnp.int32)
        _ctx_2048P = jax.random.normal(jax.random.fold_in(_rk, 11), (32, 16, 512), jnp.float32)
        _ctx_2048c = jax.random.dirichlet(jax.random.fold_in(_rk, 511), 0.3 * jnp.ones((16,), jnp.float32), (32, 361))
        _ctx_2048t = jnp.einsum('bsk,bkd->bsd', _ctx_2048c, _ctx_2048P)
        _ctx_2048t = _ctx_2048t * jax.lax.rsqrt(jnp.mean(jnp.square(_ctx_2048t)) + 1e-12) * 0.953939
        ctx_2048 = -1.52775e-05 + 0.999936 * (_ctx_2048t + 0.3 * jax.random.normal(jax.random.fold_in(_rk, 611), (32, 361, 512), jnp.float32))
        _validS = jnp.arange(100)[None, :] < _lenS[:, None]
        _validS2 = jnp.arange(361)[None, :] < _lenS2[:, None]
        _causal = jnp.tril(jnp.ones((100, 100), dtype=bool))
        mask_BxS2_ff1 = jnp.where(jnp.ones((32, 361), dtype=bool), 1.0, 0.0).astype(jnp.float32)
        _g = jax.random.normal(jax.random.fold_in(_rk, 9001), (2, 1), jnp.float32)
        _g = jnp.sign(_g) * jnp.maximum(jnp.abs(_g), 1.0) + (_g == 0) * 1.0
        g_xattn = _g[0]
        g_ffn = _g[1]
        return (x, ctx_2048, mask_BxS2_ff1, g_xattn, g_ffn)
    x, ctx_2048, mask_BxS2_ff1, g_xattn, g_ffn = _rec_inputs()

    def _L0_xattn_setup():
        import jax, jax.numpy as jnp
        import numpy as np
        H = 512
        NH = 16
        HD = H // NH
        FD = 64
        key = jax.random.key(seed)
        ks = jax.random.split(key, 12)
        B, S = (4, 1024)
        s = 1.0 / np.sqrt(H)
        sf = 1.0 / np.sqrt(HD)
        return {'query': jax.random.normal(ks[0], (B, S, H), jnp.float32), 'key': jax.random.normal(ks[1], (B, S, H), jnp.float32), 'value': jax.random.normal(ks[2], (B, S, H), jnp.float32), 'attention_mask': jnp.ones((B, S), jnp.float32), 'Wq': jax.random.normal(ks[3], (H, H), jnp.float32) * s, 'bq': jnp.zeros((H,), jnp.float32), 'Wk': jax.random.normal(ks[4], (H, H), jnp.float32) * s, 'bk': jnp.zeros((H,), jnp.float32), 'Wv': jax.random.normal(ks[5], (H, H), jnp.float32) * s, 'bv': jnp.zeros((H,), jnp.float32), 'Wqf': jax.random.normal(ks[6], (FD, HD), jnp.float32) * sf, 'Wkf': jax.random.normal(ks[7], (FD, HD), jnp.float32) * sf, 'Wo': jax.random.normal(ks[8], (H, H), jnp.float32) * s, 'bo': jnp.zeros((H,), jnp.float32)}
    _L0_xattn_all = _L0_xattn_setup()
    _L0_xattn_in = {k: v for k, v in _L0_xattn_all.items() if k in ('Wq', 'bq', 'Wk', 'bk', 'Wv', 'bv', 'Wqf', 'Wkf', 'Wo', 'bo')}
    del _L0_xattn_all

    def _L0_ffn_setup():
        import jax, jax.numpy as jnp
        import numpy as np
        EPS = 1e-05
        ACT_BITS = 8
        QB = 2 ** (ACT_BITS - 1) - 1

        def _act_quant(x):
            scale = QB / jnp.maximum(jnp.max(jnp.abs(x), axis=-1, keepdims=True), EPS)
            q = jnp.clip(jnp.round(x * scale), -QB - 1, QB) / scale
            return x + jax.lax.stop_gradient(q - x)

        def _weight_quant(w):
            scale = 1.0 / jnp.maximum(jnp.mean(jnp.abs(w)), EPS)
            q = jnp.clip(jnp.round(w * scale), -1.0, 1.0) / scale
            return w + jax.lax.stop_gradient(q - w)

        def _bitlinear(x, w):
            return jnp.einsum('bsd,od->bso', _act_quant(x), _weight_quant(w))
        key = jax.random.key(seed)
        k1, k2, k3 = jax.random.split(key, 3)
        d_model, hidden = (512, 4 * 512)
        x = jax.random.normal(k1, (2, 512, d_model), dtype=jnp.float32)
        w_norm = jnp.ones((d_model,), dtype=jnp.float32)
        w_gv = jax.random.normal(k2, (2 * hidden, d_model), dtype=jnp.float32) * 0.02
        w_out = jax.random.normal(k3, (d_model, hidden), dtype=jnp.float32) * 0.02
        return {'x': x, 'w_norm': w_norm, 'w_gv': w_gv, 'w_out': w_out}
    _L0_ffn_all = _L0_ffn_setup()
    _L0_ffn_in = {k: v for k, v in _L0_ffn_all.items() if k in ('w_norm', 'w_gv', 'w_out')}
    del _L0_ffn_all
    return {'x': x, 'ctx_2048': ctx_2048, 'mask_BxS2_ff1': mask_BxS2_ff1, 'g_xattn': g_xattn, 'g_ffn': g_ffn, 'L0_xattn_Wq': _L0_xattn_in['Wq'], 'L0_xattn_bq': _L0_xattn_in['bq'], 'L0_xattn_Wk': _L0_xattn_in['Wk'], 'L0_xattn_bk': _L0_xattn_in['bk'], 'L0_xattn_Wv': _L0_xattn_in['Wv'], 'L0_xattn_bv': _L0_xattn_in['bv'], 'L0_xattn_Wqf': _L0_xattn_in['Wqf'], 'L0_xattn_Wkf': _L0_xattn_in['Wkf'], 'L0_xattn_Wo': _L0_xattn_in['Wo'], 'L0_xattn_bo': _L0_xattn_in['bo'], 'L0_ffn_w_norm': _L0_ffn_in['w_norm'], 'L0_ffn_w_gv': _L0_ffn_in['w_gv'], 'L0_ffn_w_out': _L0_ffn_in['w_out']}

def reference(x, ctx_2048, mask_BxS2_ff1, g_xattn, g_ffn, L0_xattn_Wq, L0_xattn_bq, L0_xattn_Wk, L0_xattn_bk, L0_xattn_Wv, L0_xattn_bv, L0_xattn_Wqf, L0_xattn_Wkf, L0_xattn_Wo, L0_xattn_bo, L0_ffn_w_norm, L0_ffn_w_gv, L0_ffn_w_out):
    import jax
    import jax.numpy as jnp

    def _L0_xattn_ref(query, key, value, attention_mask, Wq, bq, Wk, bk, Wv, bv, Wqf, Wkf, Wo, bo):
        import jax, jax.numpy as jnp
        import numpy as np
        H = 512
        NH = 16
        HD = H // NH
        FD = 64
        B, Sq, _ = query.shape
        Sk = key.shape[1]

        def heads(x, W, b, S):
            return (x @ W.T + b).reshape(B, S, NH, HD).transpose(0, 2, 1, 3)
        q = heads(query, Wq, bq, Sq)
        k = heads(key, Wk, bk, Sk)
        v = heads(value, Wv, bv, Sk)
        q_prime = jax.nn.relu(jnp.einsum('bhnd,fd->bhnf', q, Wqf))
        k_prime = jax.nn.relu(jnp.einsum('bhnd,fd->bhnf', k, Wkf))
        k_prime = k_prime * attention_mask[:, None, :, None]
        kv = jnp.einsum('bhnf,bhne->bhfe', k_prime, v)
        qkv = jnp.einsum('bhmf,bhfe->bhme', q_prime, kv)
        k_sum = jnp.sum(k_prime, axis=2)
        qk_sum = jnp.einsum('bhmf,bhf->bhm', q_prime, k_sum)[..., None]
        out = qkv / (qk_sum + 1e-08)
        out = out.transpose(0, 2, 1, 3).reshape(B, Sq, H)
        return out @ Wo.T + bo

    def _L0_ffn_ref(x, w_norm, w_gv, w_out):
        import jax, jax.numpy as jnp
        import numpy as np
        EPS = 1e-05
        ACT_BITS = 8
        QB = 2 ** (ACT_BITS - 1) - 1

        def _act_quant(x):
            scale = QB / jnp.maximum(jnp.max(jnp.abs(x), axis=-1, keepdims=True), EPS)
            q = jnp.clip(jnp.round(x * scale), -QB - 1, QB) / scale
            return x + jax.lax.stop_gradient(q - x)

        def _weight_quant(w):
            scale = 1.0 / jnp.maximum(jnp.mean(jnp.abs(w)), EPS)
            q = jnp.clip(jnp.round(w * scale), -1.0, 1.0) / scale
            return w + jax.lax.stop_gradient(q - w)

        def _bitlinear(x, w):
            return jnp.einsum('bsd,od->bso', _act_quant(x), _weight_quant(w))
        residual = x
        h = x * jax.lax.rsqrt(jnp.mean(x * x, axis=-1, keepdims=True) + EPS) * w_norm
        gv = _bitlinear(h, w_gv)
        value, gate = jnp.split(gv, 2, axis=-1)
        u = value * jax.nn.silu(gate)
        out = _bitlinear(u, w_out)
        return residual + out
    x = x + jnp.tanh(g_xattn[0]) * _L0_xattn_ref(_layernorm(x, axis=-1), ctx_2048, ctx_2048, mask_BxS2_ff1, L0_xattn_Wq, L0_xattn_bq, L0_xattn_Wk, L0_xattn_bk, L0_xattn_Wv, L0_xattn_bv, L0_xattn_Wqf, L0_xattn_Wkf, L0_xattn_Wo, L0_xattn_bo)
    x = x + jnp.tanh(g_ffn[0]) * _L0_ffn_ref(_layernorm(x, axis=-1), L0_ffn_w_norm, L0_ffn_w_gv, L0_ffn_w_out)
    return x

_drawn_inputs = setup_inputs


def setup_inputs(seed=0):
    import zlib

    import numpy as np

    out = dict(_drawn_inputs(seed))
    spreads = {'L0_xattn_bq': (0.0, 0.1),
     'L0_xattn_bk': (0.0, 0.1),
     'L0_xattn_bv': (0.0, 0.1),
     'L0_xattn_bo': (0.0, 0.1),
     'L0_ffn_w_norm': (1.0, 0.2)}
    factors = {}
    for name, (base, spread) in spreads.items():
        noise = np.random.default_rng([zlib.crc32(name.encode()), seed]).standard_normal(out[name].shape)
        drawn = base * np.exp(spread * noise) if base else spread * noise
        out[name] = jnp.asarray(drawn.astype(out[name].dtype))
    for name, factor in factors.items():
        out[name] = (out[name] * factor).astype(out[name].dtype)
    return out
```

```python
from contextlib import ExitStack

import concourse.bass as bass
from concourse import mybir

F32 = mybir.dt.float32
F32R = mybir.dt.float32r
BF16 = mybir.dt.bfloat16
ALU = mybir.AluOpType
ACT = mybir.ActivationFunctionType
AX_X = mybir.AxisListType.X

P = 128
EPS = 1e-5
DEN_EPS = 1e-8
QB = 127.0
ROUND = 1.5 * 2.0 ** 23

def token_tiles(n):
    return [(s, min(P, n - s)) for s in range(0, n, P)]


def flamingo_gated_layer(nc, a, out):
    B, SQ, H = a["x"].shape
    SK = a["ctx_2048"].shape[1]
    FD, HD = a["L0_xattn_Wqf"].shape
    NH = H // HD
    KC = H // P
    HPC = P // HD
    NP = NH // 2
    TT = token_tiles(SK)
    NT = len(TT)
    GB = 4
    NG = B // GB
    GQ = GB * SQ
    SKE = SK + SK % 2
    VW = HD + 1
    F4 = HPC * FD
    HID = a["L0_ffn_w_out"].shape[1]
    assert NT == 3 and KC == 4 and NH == 16 and NG * GB == B and GQ <= 512

    ctx_dram, x_dram = a["ctx_2048"], a["x"]
    attn_dram = nc.dram_tensor("attn_scratch", (B * SQ, H), F32).ap()
    x_rows = x_dram.rearrange("b s h -> (b s) h")
    out_rows = out.rearrange("b s h -> (b s) h")

    top = ExitStack()

    def sem(name):
        return top.enter_context(nc.semaphore(name))

    with top:
        with ExitStack() as mem:
            def sb(name, shape, dt=F32):
                return mem.enter_context(nc.sbuf_tensor(name, shape, dt))

            ident = sb("ident", [P, P])
            wT = {}
            for w in ("q", "k", "v"):
                wT[w] = (sb(f"w{w}T_hi", [P, KC, H], F32R), sb(f"w{w}T_lo", [P, KC, H], F32R))
            bd = {w: (sb(f"bd{w}_hi", [P, F4], F32R), sb(f"bd{w}_lo", [P, F4], F32R)) for w in "qk"}
            fmap_nat = sb("fmap_nat", [FD, 2, P])
            bias_col = sb("bias_col", [P, 2, KC])
            bv_bc = sb("bv_bc", [P, H])
            mask_nat = sb("mask_nat", [B, SK])
            maskT = sb("maskT", [P, NT, B])
            mask_cur = sb("mask_cur", [P, 2, NT])
            ctx_nat = sb("ctx_nat", [P, 2, NT, H])
            ctxT = [(sb(f"ctxT{i}_hi", [P, KC, SKE], F32R), sb(f"ctxT{i}_lo", [P, KC, SKE], F32R)) for i in range(2)]
            kT = (sb("kT_hi", [P, KC, SK], F32R), sb("kT_lo", [P, KC, SK], F32R))
            kmap = sb("kmap", [P, NT, NH * FD])
            vones = sb("vones", [P, NT, NH, VW])
            x_nat = sb("x_nat", [P, GB, H])
            x_stat = sb("x_stat", [P, GB, 6])
            x_mv = sb("x_mv", [P, GB, 2])
            x_rstd = sb("x_rstd", [P, 2, GB])
            minus_half = sb("minus_half", [P, GB])
            carried = sb("carried", [P, 2])
            xT = (sb("xT_hi", [P, KC, GQ], F32R), sb("xT_lo", [P, KC, GQ], F32R))
            qT = (sb("qT_hi", [P, KC, GQ], F32R), sb("qT_lo", [P, KC, GQ], F32R))
            qmap = sb("qmap", [P, NP, GQ])
            kvT = sb("kvT", [P, NP * FD])
            kvbd = sb("kvbd", [P, NP, 2 * VW])
            attn_sb = sb("attn_sb", [P, 2, H])
            den = sb("den", [P, 2, 2, NH // 2])

            bank = [mem.enter_context(nc.psum_tensor(f"bank{i}", [P, 512], F32)) for i in range(8)]
            T_BANKS, K_BANKS, V_BANKS = (0, 1), (2, 3), (4, 5)
            KV_BANK, KVT_BANK = 6, 7
            ATTN_BANKS = (6, 7)

            small_ld, wq_ld, wk_ld, wv_ld, x_ld = (sem(n) for n in ("small_ld", "wq_ld", "wk_ld", "wv_ld", "x_ld"))
            ctx_ld = [sem(f"ctx_ld{i}") for i in range(2)]
            attn_st = [sem(f"attn_st{i}") for i in range(2)]
            ident_ok, zeros_ok, zeroed = sem("ident_ok"), sem("zeros_ok"), sem("zeroed")
            setup_t, setup_hi, setup_lo = sem("setup_t"), sem("setup_hi"), sem("setup_lo")
            ctx_t, x_t, kt_mm, qt_mm, v_mm, kmap_mm, qmap_mm, kv_mm, kvt_t, attn_mm = (sem(n) for n in (
                "ctx_t", "x_t", "kt_mm", "qt_mm", "v_mm", "kmap_mm", "qmap_mm", "kv_mm", "kvt_t", "attn_mm"))
            ctx_hi, x_hi, kt_hi, qt_hi, qmap_ok, kv_top, kvbd_top = (sem(n) for n in (
                "ctx_hi", "x_hi", "kt_hi", "qt_hi", "qmap_ok", "kv_top", "kvbd_top"))
            ctx_lo, x_lo, kt_lo, qt_lo, v_ok, kmap_ok, kv_bot, kvbd_bot, attn_ok, ln_step, xhat_ok, den_step = (
                sem(n) for n in ("ctx_lo", "x_lo", "kt_lo", "qt_lo", "v_ok", "kmap_ok", "kv_bot", "kvbd_bot",
                                 "attn_ok", "ln_step", "xhat_ok", "den_step"))
            mask_ok, rstd_ok = sem("mask_ok"), sem("rstd_ok")

            T_RING = ([("ctx", 0, j) for j in range(NT)] + [("ctx", 1, j) for j in range(NT)]
                      + [("x", 0, r) for r in range(GB)]
                      + [("ctx", r + 1, j) for r in range(1, GB - 1) for j in range(NT)])
            K_RING = ([("kt", 0, c) for c in range(KC)] + [("qt", 0, c) for c in range(KC)]
                      + [("kt", r, c) for r in range(1, GB) for c in range(KC)])
            V_RING = []
            for r in range(GB):
                V_RING += [("v", r, j) for j in range(NT)] + [("kmap", r, i) for i in range(2 * NT)]
                V_RING += [("qmap", 0, p) for p in range(NP)] if r == 0 else []
            assert not len(T_RING) % 2 and not len(K_RING) % 2 and not len(V_RING) % 2
            EMPTIED = {
                "ctx": lambda g, r, i: (ctx_lo, (g * GB + r) * NT + i + 1),
                "x": lambda g, r, i: (x_lo, g * GB + i + 1),
                "kt": lambda g, r, i: (kt_lo, (g * GB + r) * KC + i + 1),
                "qt": lambda g, r, i: (qt_lo, g * KC + i + 1),
                "v": lambda g, r, i: (v_ok, (g * GB + r) * NT + i + 1),
                "kmap": lambda g, r, i: (kmap_ok, (g * GB + r) * 2 * NT + i + 1),
                "qmap": lambda g, r, i: (qmap_ok, g * NP + i + 1),
            }

            def take_bank(pe, ring, banks, g, job, setup_jobs=0):
                n = ring.index(job)
                if n >= 2:
                    kind, r, i = ring[n - 2]
                    pe.wait_ge(*EMPTIED[kind](g, r, i))
                elif not (isinstance(g, int) and g == 0):
                    kind, r, i = ring[n - 2]
                    pe.wait_ge(*EMPTIED[kind](g - 1, r, i))
                elif setup_jobs:
                    pe.wait_ge(setup_lo, setup_jobs)
                return bank[banks[n % 2]]

            SETUP_W = [("k", kmap[:].rearrange("p t f -> p (t f)"), wk_ld),
                       ("v", qmap[:].rearrange("p n t -> p (n t)"), wv_ld),
                       ("q", x_nat[:].rearrange("p r h -> p (r h)"), wq_ld)]

            def w_nat(flat):
                return flat[:, 0:KC * H].rearrange("p (m i) -> p m i", m=KC)

            SETUP_JOBS = 3 * KC + 3

            def block_diagonal(eng, u):
                rows = slice(u * FD, (u + 1) * FD)
                src = bank[KVT_BANK][rows, :].rearrange("p (j h e) -> p h j e", j=NP // 2, h=2)[:, :, :, 0:VW]
                dst = kvbd[rows, :, u * VW:(u + 1) * VW].rearrange("p (h j) e -> p h j e", h=2)
                if u == 0:
                    return nc.scalar.activation(dst, src, ACT.Copy)
                return nc.vector.tensor_copy(dst, src)

            with nc.Block() as block:
                @block.sync
                def _(sp):
                    def load_ctx(g, r):
                        b = g * GB + r
                        if not (isinstance(g, int) and g == 0 and r < 2):
                            sp.wait_ge(ctx_t, (b - 1) * NT)
                        dst, src = ctx_nat[:, r % 2], ctx_dram[b]
                        full = NT - 1
                        sp.dma_start(dst[:, 0:full, :], src[0:full * P, :].rearrange("(j p) d -> p j d", p=P)
                                     ).then_inc(ctx_ld[r % 2], 16)
                        sp.dma_start(dst[0:TT[-1][1], full, :], src[full * P:SK, :]).then_inc(ctx_ld[r % 2], 16)

                    def load_x(g):
                        if isinstance(g, int) and g == 0:
                            sp.wait_ge(setup_t, 3 * KC)
                        else:
                            sp.wait_ge(x_t, g * GB)
                        sp.dma_start(x_nat[0:SQ, :, :], x_dram[bass.ds(g * GB, GB)].rearrange("r p d -> p r d")
                                     ).then_inc(x_ld, 16)

                    def store_attn(g, r):
                        b = g * GB + r - 1
                        sp.wait_ge(attn_ok, 2 * b + 2)
                        sp.dma_start(attn_dram[bass.ds(b * SQ, SQ), :], attn_sb[0:SQ, (r - 1) % 2, :]
                                     ).then_inc(attn_st[(r - 1) % 2], 16)

                    sp.dma_start(w_nat(SETUP_W[0][1]), a["L0_xattn_Wk"].rearrange("(m p) i -> p m i", p=P)).then_inc(wk_ld, 16)
                    load_ctx(0, 0)
                    sp.dma_start(w_nat(SETUP_W[1][1]), a["L0_xattn_Wv"].rearrange("(m p) i -> p m i", p=P)).then_inc(wv_ld, 16)
                    sp.dma_start(w_nat(SETUP_W[2][1]), a["L0_xattn_Wq"].rearrange("(m p) i -> p m i", p=P)).then_inc(wq_ld, 16)

                    def group(g, first, last):
                        load_ctx(g, 2)
                        if not first:
                            store_attn(g, 0)
                        load_ctx(g, 3)
                        if not last:
                            load_x(g + 1)
                            load_ctx(g + 1, 0)
                        store_attn(g, 1)
                        if not last:
                            load_ctx(g + 1, 1)
                        store_attn(g, 2)
                        store_attn(g, 3)

                    load_x(0)
                    load_ctx(0, 1)
                    group(0, True, False)
                    with sp.Fori(1, NG - 1) as g:
                        group(g, False, False)
                    group(NG - 1, False, True)
                    store_attn(NG, 0)
                    for i in range(2):
                        sp.wait_ge(attn_st[i], 16 * B // 2)

                @block.gpsimd
                def _(pool):
                    pool.memset(ident[:], 1.0).then_inc(ident_ok, 1)
                    pool.wait_ge(ident_ok, 1)
                    pool.affine_select(out=ident[:], in_=ident[:], compare_op=ALU.is_equal, fill=0.0, base=0,
                                       pattern=[[-1, P]], channel_multiplier=1).then_inc(ident_ok, 1)
                    pool.memset(vones[:, :, :, HD:VW], 1.0).then_inc(zeroed, 1)
                    pool.memset(kvT[:], 0.0).then_inc(zeroed, 1)
                    pool.memset(kvbd[:], 0.0).then_inc(zeroed, 1)
                    pool.memset(minus_half[:], -0.5).then_inc(zeroed, 1)
                    pool.memset(carried[:], 0.0).then_inc(zeroed, 1)

                    def mask_column(g, r):
                        b = g * GB + r
                        if isinstance(g, int) and g == 0 and r == 0:
                            pool.wait_ge(setup_lo, SETUP_JOBS)
                        if not (isinstance(g, int) and g == 0 and r < 2):
                            pool.wait_ge(kmap_ok, (b - 1) * 2 * NT)
                        pool.tensor_copy(mask_cur[:, r % 2, :], maskT[:, :, bass.ds(b, 1)].rearrange("p t o -> p (t o)")
                                         ).then_inc(mask_ok, 1)

                    def group(g):
                        mask_column(g, 0)
                        pool.wait_ge(ln_step, g * (GB + 2) + GB + 2)
                        if isinstance(g, int):
                            pool.wait_ge(zeroed, 5 + 4 * (SKE - SK))
                        pool.tensor_tensor(x_rstd[0:SQ, 1, :], x_rstd[0:SQ, 0, :], minus_half[0:SQ, :], ALU.pow
                                           ).then_inc(rstd_ok, 1)
                        for r in range(1, GB):
                            mask_column(g, r)

                    group(0)
                    with pool.Fori(1, NG) as g:
                        group(g)

                @block.scalar
                def _(act):
                    act.dma_start(mask_nat[:], a["mask_BxS2_ff1"]).then_inc(small_ld, 16)
                    for i, n in enumerate(("L0_xattn_Wqf", "L0_xattn_Wkf")):
                        for h in range(HPC):
                            act.dma_start(fmap_nat[:, i, h * HD:(h + 1) * HD], a[n]).then_inc(small_ld, 16)
                    for i, n in enumerate(("L0_xattn_bq", "L0_xattn_bk")):
                        act.dma_start(bias_col[:, i, :], a[n].rearrange("(c p) -> p c", p=P),
                                      allow_slow_non_contiguous=True).then_inc(small_ld, 16)
                    act.dma_start(bv_bc[:], a["L0_xattn_bv"].partition_broadcast(P)).then_inc(small_ld, 16)

                    n = 0
                    for w, _, _ in SETUP_W:
                        for m in range(KC):
                            act.wait_ge(setup_t, n + 1)
                            nc.scalar.activation(wT[w][0][:, :, m * P:(m + 1) * P],
                                                 bank[T_BANKS[n % 2]][:].rearrange("p (c o) -> p c o", c=KC),
                                                 ACT.Copy).then_inc(setup_hi, 1)
                            n += 1
                    act.wait_ge(zeros_ok, 4)
                    for w in "qk":
                        act.wait_ge(setup_t, n + 1)
                        for h in range(HPC):
                            last = nc.scalar.activation(bd[w][0][h * HD:(h + 1) * HD, h * FD:(h + 1) * FD],
                                                        bank[T_BANKS[n % 2]][h * HD:(h + 1) * HD, 0:FD], ACT.Copy)
                        last.then_inc(setup_hi, 1)
                        n += 1

                    def hi_ctx(g, r):
                        b = g * GB + r
                        if not (isinstance(g, int) and g == 0 and r < 2):
                            act.wait_ge(v_mm, (b - 1) * NT)
                        for j, (t0, n) in enumerate(TT):
                            act.wait_ge(ctx_t, b * NT + j + 1)
                            src = bank[T_BANKS[T_RING.index(("ctx", r, j)) % 2]]
                            nc.scalar.activation(ctxT[r % 2][0][:, :, t0:t0 + n],
                                                 src[:].rearrange("p (c t) -> p c t", c=KC)[:, :, 0:n], ACT.Copy
                                                 ).then_inc(ctx_hi, 1)

                    def group(g, first):
                        for r in range(GB):
                            b = g * GB + r
                            if r == 0:
                                hi_ctx(g, 0)
                            if not (first and r == 0):
                                act.wait_ge(kv_mm, b)
                                nc.scalar.activation(kvT[0:VW, :], bank[KV_BANK][0:VW, :], ACT.Copy).then_inc(kv_top, 1)
                            for c in range(KC):
                                act.wait_ge(kt_mm, b * KC + c + 1)
                                src = bank[K_BANKS[K_RING.index(("kt", r, c)) % 2]]
                                nc.scalar.activation(kT[0][:, c, :], src[:, 0:SK], ACT.Identity,
                                                     bias=bias_col[:, 1, c:c + 1]).then_inc(kt_hi, 1)
                            if r < GB - 1:
                                hi_ctx(g, r + 1)
                            if r == 0:
                                for i in range(GB):
                                    act.wait_ge(x_t, g * GB + i + 1)
                                    src = bank[T_BANKS[T_RING.index(("x", 0, i)) % 2]]
                                    nc.scalar.activation(xT[0][:, :, i * SQ:(i + 1) * SQ],
                                                         src[:].rearrange("p (c t) -> p c t", c=KC)[:, :, 0:SQ], ACT.Copy
                                                         ).then_inc(x_hi, 1)
                                for c in range(KC):
                                    act.wait_ge(qt_mm, g * KC + c + 1)
                                    src = bank[K_BANKS[K_RING.index(("qt", 0, c)) % 2]]
                                    nc.scalar.activation(qT[0][:, c, :], src[:, 0:GQ], ACT.Identity,
                                                         bias=bias_col[:, 0, c:c + 1]).then_inc(qt_hi, 1)
                            if not (first and r == 0):
                                act.wait_ge(kvt_t, b)
                                block_diagonal(act, 0).then_inc(kvbd_top, 1)
                            if r == 0:
                                for p in range(NP):
                                    act.wait_ge(qmap_mm, g * NP + p + 1)
                                    src = bank[V_BANKS[V_RING.index(("qmap", 0, p)) % 2]]
                                    nc.scalar.activation(qmap[:, p, :], src[:, 0:GQ], ACT.Relu).then_inc(qmap_ok, 1)

                    group(0, True)
                    with act.Fori(1, NG) as g:
                        group(g, False)
                    act.wait_ge(kv_mm, B)
                    nc.scalar.activation(kvT[0:VW, :], bank[KV_BANK][0:VW, :], ACT.Copy).then_inc(kv_top, 1)
                    act.wait_ge(kvt_t, B)
                    block_diagonal(act, 0).then_inc(kvbd_top, 1)

                @block.vector
                def _(dve):
                    for w in "qk":
                        for part in range(2):
                            nc.vector.memset(bd[w][part][:].bitcast(F32), 0.0).then_inc(zeros_ok, 1)
                    nc.vector.memset(maskT[:], 0.0).then_inc(zeros_ok, 1)
                    if SKE > SK:
                        for pair in ctxT:
                            for part in pair:
                                nc.vector.memset(part[:, :, SK:SKE].bitcast(F32), 0.0).then_inc(zeroed, 1)

                    n = 0
                    for w, _, _ in SETUP_W:
                        for m in range(KC):
                            dve.wait_ge(setup_hi, n + 1)
                            hi, lo = (t[:, :, m * P:(m + 1) * P] for t in wT[w])
                            nc.vector.tensor_tensor(lo, bank[T_BANKS[n % 2]][:].rearrange("p (c o) -> p c o", c=KC),
                                                    hi.bitcast(F32), ALU.subtract).then_inc(setup_lo, 1)
                            n += 1
                    dve.wait_ge(zeros_ok, 5)
                    for w in "qk":
                        dve.wait_ge(setup_hi, n + 1)
                        for h in range(HPC):
                            at = (slice(h * HD, (h + 1) * HD), slice(h * FD, (h + 1) * FD))
                            last = nc.vector.tensor_tensor(bd[w][1][at], bank[T_BANKS[n % 2]][at[0], 0:FD],
                                                           bd[w][0][at].bitcast(F32), ALU.subtract)
                        last.then_inc(setup_lo, 1)
                        n += 1
                    dve.wait_ge(setup_t, n + 1)
                    src = bank[T_BANKS[n % 2]][:, 0:NT * B].rearrange("p (j b) -> p j b", j=NT)
                    nc.vector.tensor_copy(maskT[:, 0:NT - 1, :], src[:, 0:NT - 1, :])
                    nc.vector.tensor_copy(maskT[0:TT[-1][1], NT - 1, :], src[0:TT[-1][1], NT - 1, :]).then_inc(setup_lo, 1)
                    dve.wait_ge(small_ld, 16 * 12)
                    dve.wait_ge(zeroed, 5 + 4 * (SKE - SK))

                    def lo_ctx(g, r):
                        b = g * GB + r
                        for j, (t0, n) in enumerate(TT):
                            dve.wait_ge(ctx_hi, b * NT + j + 1)
                            src = bank[T_BANKS[T_RING.index(("ctx", r, j)) % 2]]
                            hi, lo = (t[:, :, t0:t0 + n] for t in ctxT[r % 2])
                            nc.vector.tensor_tensor(lo, src[:].rearrange("p (c t) -> p c t", c=KC)[:, :, 0:n],
                                                    hi.bitcast(F32), ALU.subtract).then_inc(ctx_lo, 1)

                    def carrier():
                        nc.vector.tensor_copy(carried[:, 1:2], carried[:, 0:1])

                    def layernorm(g):
                        base = g * (GB + 2)
                        dve.wait_ge(x_ld, (g + 1) * 16)
                        for i in range(GB):
                            nc.vector.bn_stats(x_stat[0:SQ, i, :], x_nat[0:SQ, i, :]).then_inc(ln_step, 1)
                        for i in range(GB):
                            if i == 0:
                                dve.wait_ge(ln_step, base + GB)
                                carrier()
                            last = nc.vector.bn_aggr(x_mv[0:SQ, i, :], x_stat[0:SQ, i, :])
                        last.then_inc(ln_step, 1)
                        dve.wait_ge(ln_step, base + GB + 1)
                        nc.vector.tensor_scalar(x_rstd[0:SQ, 0, :], x_mv[0:SQ, :, 1], EPS, None, ALU.add
                                                ).then_inc(ln_step, 1)
                        dve.wait_ge(rstd_ok, g + 1)
                        for i in range(GB):
                            nc.vector.tensor_scalar(x_nat[0:SQ, i, :], x_nat[0:SQ, i, :], x_mv[0:SQ, i, 0:1],
                                                    x_rstd[0:SQ, 1, i:i + 1], ALU.subtract, ALU.mult).then_inc(xhat_ok, 1)

                    def attn_out(g, r):
                        b, par = g * GB + r - 1, (r - 1) % 2
                        if not (isinstance(g, int) and (g == 0 and r < 3)):
                            dve.wait_ge(attn_st[par], (g * (GB // 2) + (r - 1 - par) // 2) * 16)
                        for w in range(2):
                            dve.wait_ge(attn_mm, 2 * b + w + 1)
                            src = bank[ATTN_BANKS[w]][0:SQ, 0:NP * VW].rearrange("p (h e) -> p h e", e=VW)
                            d0, d1 = den[0:SQ, w, 0, :], den[0:SQ, w, 1, :]
                            nc.vector.tensor_scalar(d0, src[:, :, HD], DEN_EPS, None, ALU.add).then_inc(den_step, 1)
                            dve.wait_ge(den_step, 4 * b + 2 * w + 1)
                            nc.vector.reciprocal(d1, d0).then_inc(den_step, 1)
                            dve.wait_ge(den_step, 4 * b + 2 * w + 2)
                            nc.vector.tensor_tensor(
                                attn_sb[0:SQ, par, w * NP * HD:(w + 1) * NP * HD].rearrange("p (h e) -> p h e", e=HD),
                                src[:, :, 0:HD], d1.unsqueeze(2).to_broadcast((SQ, NP, HD)), ALU.mult).then_inc(attn_ok, 1)

                    def group(g, first):
                        for r in range(GB):
                            b = g * GB + r
                            if r == 0:
                                lo_ctx(g, 0)
                                layernorm(g)
                            if not (first and r == 0):
                                dve.wait_ge(kv_mm, b)
                                nc.vector.tensor_copy(kvT[FD:FD + VW, :], bank[KV_BANK][FD:FD + VW, :]).then_inc(kv_bot, 1)
                            for c in range(KC):
                                dve.wait_ge(kt_hi, b * KC + c + 1)
                                src = bank[K_BANKS[K_RING.index(("kt", r, c)) % 2]]
                                nc.vector.scalar_tensor_tensor(kT[1][:, c, :], src[:, 0:SK], bias_col[:, 1, c:c + 1],
                                                               kT[0][:, c, :].bitcast(F32), ALU.add, ALU.subtract
                                                               ).then_inc(kt_lo, 1)
                            if r < GB - 1:
                                lo_ctx(g, r + 1)
                            if r == 0:
                                for i in range(GB):
                                    dve.wait_ge(x_hi, g * GB + i + 1)
                                    src = bank[T_BANKS[T_RING.index(("x", 0, i)) % 2]]
                                    hi, lo = (t[:, :, i * SQ:(i + 1) * SQ] for t in xT)
                                    nc.vector.tensor_tensor(lo, src[:].rearrange("p (c t) -> p c t", c=KC)[:, :, 0:SQ],
                                                            hi.bitcast(F32), ALU.subtract).then_inc(x_lo, 1)
                            for j, (t0, n) in enumerate(TT):
                                dve.wait_ge(v_mm, b * NT + j + 1)
                                src = bank[V_BANKS[V_RING.index(("v", r, j)) % 2]]
                                nc.vector.tensor_tensor(vones[0:n, j, :, 0:HD], src[0:n, :].rearrange("p (h e) -> p h e", e=HD),
                                                        bv_bc[0:n, :].rearrange("p (h e) -> p h e", e=HD), ALU.add
                                                        ).then_inc(v_ok, 1)
                            if r == 0:
                                for c in range(KC):
                                    dve.wait_ge(qt_hi, g * KC + c + 1)
                                    src = bank[K_BANKS[K_RING.index(("qt", 0, c)) % 2]]
                                    nc.vector.scalar_tensor_tensor(qT[1][:, c, :], src[:, 0:GQ], bias_col[:, 0, c:c + 1],
                                                                   qT[0][:, c, :].bitcast(F32), ALU.add, ALU.subtract
                                                                   ).then_inc(qt_lo, 1)
                            if not (first and r == 0):
                                dve.wait_ge(kvt_t, b)
                                block_diagonal(dve, 1).then_inc(kvbd_bot, 1)
                            dve.wait_ge(mask_ok, b + 1)
                            for i in range(2 * NT):
                                j, half = divmod(i, 2)
                                n = TT[j][1]
                                dve.wait_ge(kmap_mm, b * 2 * NT + i + 1)
                                src = bank[V_BANKS[V_RING.index(("kmap", r, i)) % 2]]
                                nc.vector.tensor_scalar(kmap[0:n, j, half * 512:(half + 1) * 512], src[0:n, :], 0.0,
                                                        mask_cur[0:n, r % 2, j:j + 1], ALU.max, ALU.mult
                                                        ).then_inc(kmap_ok, 1)
                            if not (first and r == 0):
                                attn_out(g, r)

                    group(0, True)
                    with dve.Fori(1, NG) as g:
                        group(g, False)
                    dve.wait_ge(kv_mm, B)
                    nc.vector.tensor_copy(kvT[FD:FD + VW, :], bank[KV_BANK][FD:FD + VW, :]).then_inc(kv_bot, 1)
                    dve.wait_ge(kvt_t, B)
                    block_diagonal(dve, 1).then_inc(kvbd_bot, 1)
                    attn_out(NG, 0)

                @block.tensor
                def _(pe):
                    def split_matmul(out_, steps):
                        for k, ((lh, ll), (rh, rl)) in enumerate(steps):
                            nc.tensor.matmul(out_, lh, rh, start=(k == 0), stop=False)
                            nc.tensor.matmul(out_, lh, rl, start=False, stop=False)
                            last = nc.tensor.matmul(out_, ll, rh, start=False, stop=(k == len(steps) - 1))
                        return last

                    def cut(pair, *at):
                        return tuple(t[at] for t in pair)

                    pe.wait_ge(ident_ok, 2)
                    n = 0
                    for w, flat, loaded in SETUP_W:
                        pe.wait_ge(loaded, 16)
                        for m in range(KC):
                            if n >= 2:
                                pe.wait_ge(setup_lo, n - 1)
                            for c in range(KC):
                                last = nc.tensor.transpose(bank[T_BANKS[n % 2]][:, c * P:(c + 1) * P],
                                                           w_nat(flat)[:, m, c * P:(c + 1) * P], ident[:])
                            last.then_inc(setup_t, 1)
                            n += 1
                    pe.wait_ge(small_ld, 16 * 12)
                    for i in range(2):
                        pe.wait_ge(setup_lo, n - 1)
                        nc.tensor.transpose(bank[T_BANKS[n % 2]][:, 0:FD], fmap_nat[:, i, :], ident[0:FD, 0:FD]
                                            ).then_inc(setup_t, 1)
                        n += 1
                    pe.wait_ge(setup_lo, n - 1)
                    for j, (t0, tn) in enumerate(TT):
                        last = nc.tensor.transpose(bank[T_BANKS[n % 2]][0:tn, j * B:(j + 1) * B],
                                                   mask_nat[:, t0:t0 + tn], ident[0:B, 0:B])
                    last.then_inc(setup_t, 1)

                    def transpose_ctx(g, r):
                        b = g * GB + r
                        pe.wait_ge(ctx_ld[r % 2], (g * (GB // 2) + r // 2 + 1) * 32)
                        for j, (t0, n) in enumerate(TT):
                            dst = take_bank(pe, T_RING, T_BANKS, g, ("ctx", r, j), SETUP_JOBS)
                            for c in range(KC):
                                last = nc.tensor.transpose(dst[:, c * P:c * P + n],
                                                           ctx_nat[0:n, r % 2, j, c * P:(c + 1) * P], ident[0:n, 0:n])
                            last.then_inc(ctx_t, 1)

                    def kv(b):
                        pe.wait_ge(kmap_ok, (b + 1) * 2 * NT)
                        pe.wait_ge(v_ok, (b + 1) * NT)
                        if not (isinstance(b, int) and b == 0):
                            pe.wait_ge(attn_ok, 2 * b - 1)
                        for h in range(NH):
                            u, s = divmod(h, NP)
                            for j, (t0, n) in enumerate(TT):
                                last = nc.tensor.matmul(bank[KV_BANK][u * FD:u * FD + VW, s * FD:(s + 1) * FD],
                                                        vones[0:n, j, h, :], kmap[0:n, j, h * FD:(h + 1) * FD],
                                                        start=(j == 0), stop=(j == NT - 1))
                        last.then_inc(kv_mm, 1)

                    def transpose_kv(b):
                        pe.wait_ge(kv_top, b + 1)
                        pe.wait_ge(kv_bot, b + 1)
                        if not (isinstance(b, int) and b == 0):
                            pe.wait_ge(attn_ok, 2 * b)
                        for j in range(NP // 2):
                            last = nc.tensor.transpose(bank[KVT_BANK][:, j * P:(j + 1) * P], kvT[:, j * P:(j + 1) * P], ident[:])
                        last.then_inc(kvt_t, 1)

                    def attend(b, r):
                        pe.wait_ge(kvbd_top, b + 1)
                        pe.wait_ge(kvbd_bot, b + 1)
                        for p in range(NP):
                            w, i = divmod(p, NP // 2)
                            last = nc.tensor.matmul(bank[ATTN_BANKS[w]][0:SQ, i * 2 * VW:(i + 1) * 2 * VW],
                                                    qmap[:, p, r * SQ:(r + 1) * SQ], kvbd[:, p, :], start=True, stop=True)
                            if i == NP // 2 - 1:
                                last.then_inc(attn_mm, 1)

                    def group(g, first):
                        for r in range(GB):
                            b = g * GB + r
                            cT = ctxT[r % 2]
                            if r == 0:
                                transpose_ctx(g, 0)
                            if not (first and r == 0):
                                kv(b - 1)
                            pe.wait_ge(ctx_lo, (b + 1) * NT)
                            for m in range(KC):
                                dst = take_bank(pe, K_RING, K_BANKS, g, ("kt", r, m))
                                split_matmul(dst[:, 0:SKE], [(cut(wT["k"], slice(None), c, slice(m * P, (m + 1) * P)),
                                                             cut(cT, slice(None), c, slice(None))) for c in range(KC)]
                                             ).then_inc(kt_mm, 1)
                            if r < GB - 1:
                                transpose_ctx(g, r + 1)
                            if r == 0:
                                for i in range(GB):
                                    pe.wait_ge(xhat_ok, g * GB + i + 1)
                                    dst = take_bank(pe, T_RING, T_BANKS, g, ("x", 0, i))
                                    for c in range(KC):
                                        last = nc.tensor.transpose(dst[:, c * P:c * P + SQ],
                                                                   x_nat[0:SQ, i, c * P:(c + 1) * P], ident[0:SQ, 0:SQ])
                                    last.then_inc(x_t, 1)
                            for j, (t0, n) in enumerate(TT):
                                dst = take_bank(pe, V_RING, V_BANKS, g, ("v", r, j))
                                split_matmul(dst[0:n, :], [(cut(cT, slice(None), c, slice(t0, t0 + n)),
                                                            cut(wT["v"], slice(None), c, slice(None))) for c in range(KC)]
                                             ).then_inc(v_mm, 1)
                            if r == 0:
                                pe.wait_ge(x_lo, (g + 1) * GB)
                                for m in range(KC):
                                    dst = take_bank(pe, K_RING, K_BANKS, g, ("qt", 0, m))
                                    split_matmul(dst[:, 0:GQ], [(cut(wT["q"], slice(None), c, slice(m * P, (m + 1) * P)),
                                                                 cut(xT, slice(None), c, slice(None))) for c in range(KC)]
                                                 ).then_inc(qt_mm, 1)
                            if not (first and r == 0):
                                transpose_kv(b - 1)
                            for i in range(2 * NT):
                                j, half = divmod(i, 2)
                                t0, n = TT[j]
                                dst = take_bank(pe, V_RING, V_BANKS, g, ("kmap", r, i))
                                if i == 0:
                                    pe.wait_ge(kt_lo, (b + 1) * KC)
                                for cc in range(2):
                                    c = 2 * half + cc
                                    last = split_matmul(dst[0:n, cc * F4:(cc + 1) * F4],
                                                        [(cut(kT, slice(None), c, slice(t0, t0 + n)), cut(bd["k"], slice(None)))])
                                last.then_inc(kmap_mm, 1)
                            if r == 1:
                                pe.wait_ge(qmap_ok, (g + 1) * NP)
                            if not (first and r == 0):
                                attend(b - 1, (r - 1) % GB)
                            if r == 0:
                                pe.wait_ge(qt_lo, (g + 1) * KC)
                                for p in range(NP):
                                    c, s = divmod(p, 2)
                                    dst = take_bank(pe, V_RING, V_BANKS, g, ("qmap", 0, p))
                                    split_matmul(dst[:, 0:GQ], [(cut(bd["q"], slice(None), slice(s * P, (s + 1) * P)),
                                                                 cut(qT, slice(None), c, slice(None)))]).then_inc(qmap_mm, 1)

                    pe.wait_ge(setup_lo, SETUP_JOBS)
                    pe.wait_ge(zeroed, 5 + 4 * (SKE - SK))
                    group(0, True)
                    with pe.Fori(1, NG) as g:
                        group(g, False)
                    kv(B - 1)
                    transpose_kv(B - 1)
                    attend(B - 1, GB - 1)

        ffn(nc, a, top, x_rows, attn_dram, out_rows)


def ffn(nc, a, top, x_rows, attn_dram, out_rows):
    N, H = x_rows.shape
    HID = a["L0_ffn_w_out"].shape[1]
    KC, HC = H // P, HID // P
    NTILE = N // P
    CH = HID
    GVC = 2 * HID * H // (P * CH)
    OUTC = HID * H // (P * CH)
    NCH = GVC + OUTC
    JB = HID // 512
    UN = 4
    assert N % P == 0 and CH == 4 * H and JB == 4

    def sem(name):
        return top.enter_context(nc.semaphore(name))

    with ExitStack() as mem:
        def sb(name, shape, dt=F32):
            return mem.enter_context(nc.sbuf_tensor(name, shape, dt))

        identf, identb = sb("identf", [P, P]), sb("identb", [P, P], BF16)
        ones = sb("ones", [P, P])
        woT = (sb("woT_hi", [P, KC, H], F32R), sb("woT_lo", [P, KC, H], F32R))
        wgvT = sb("wgvT", [P, KC, 2 * HID], BF16)
        woutT = sb("woutT", [P, HC, H], BF16)
        stage = sb("stage", [P, 3, CH])
        tern = sb("tern", [P, 2, CH])
        ternb = sb("ternb", [P, 2, CH], BF16)
        abs_sum = sb("abs_sum", [P, NCH])
        wstat = sb("wstat", [P, 2, 4])
        gates = sb("gates", [P, 4])
        bo_bc, wn_bc = sb("bo_bc", [P, H]), sb("wn_bc", [P, H])
        minus_half = sb("minus_half2", [P, 1])
        carried = sb("carried2", [P, 2])

        attn_in, x_in = sb("attn_in", [P, 2, H]), sb("x_in", [P, 2, H])
        aT = (sb("aT_hi", [P, KC, P], F32R), sb("aT_lo", [P, KC, P], F32R))
        xb = sb("xb", [P, H])
        x1, y = sb("x1", [P, H]), sb("y", [P, H])
        base = sb("base", [P, UN, H])
        h, hround, hq = sb("h", [P, H]), sb("hround", [P, H]), sb("hq", [P, H], BF16)
        hT = sb("hT", [P, KC, P], BF16)
        bn, mv = sb("bn", [P, 6]), sb("mv", [P, 2])
        rs = sb("rs", [P, 2, 4])
        hs = sb("hs", [P, 4])
        c1 = sb("c1", [P, UN])
        sg = sb("sg", [P, 2, 512])
        u, uround, uq = sb("u", [P, HID]), sb("uround", [P, HID]), sb("uq", [P, HID], BF16)
        uT = sb("uT", [P, HC, P], BF16)
        um = sb("um", [P, JB])
        us = sb("us", [P, 4])
        c2 = sb("c2", [P, UN])
        o_sb = sb("o_sb", [P, 2, H])

        bank = [mem.enter_context(nc.psum_tensor(f"fbank{i}", [P, 512], F32)) for i in range(8)]
        AT, WO, OUT, QT = 0, 1, 6, 7
        GV = ((2, 3), (4, 5))
        W_BANKS = (2, 3, 4, 5)

        small_ld, wo_ld = sem("fsmall_ld"), sem("wo_ld")
        w_ld = [sem(f"w_ld{i}") for i in range(3)]
        const_ok, ident_ok = sem("const_ok"), sem("fident_ok")
        asum_ok, wsum_mm, wstat_step, tern_step, ternb_ok, w_t, w_ok0, w_ok1 = (sem(n) for n in (
            "asum_ok", "wsum_mm", "wstat_step", "tern_step", "ternb_ok", "w_t", "w_ok0", "w_ok1"))
        wo_t, wo_hi, wo_lo, tanh_ok, bo_ok = (sem(n) for n in ("wo_t", "wo_hi", "wo_lo", "tanh_ok", "bo_ok"))
        tile_ld = [sem(f"tile_ld{i}") for i in range(2)]
        out_st = [sem(f"out_st{i}") for i in range(2)]
        at_t, wo_mm, h_t, gv_mm, u_t, out_mm = (sem(n) for n in ("at_t", "wo_mm", "h_t", "gv_mm", "u_t", "out_mm"))
        at_hi, hT_ok, sg_ok, sq_ok, uq_ok, uT_ok = (sem(n) for n in ("at_hi", "hT_ok", "sg_ok", "sq_ok", "uq_ok", "uT_ok"))
        at_lo, ln, hq_ok, c1_ok, u_ok, um_step, us_ok, c2_ok, base_ok, o_ok = (sem(n) for n in (
            "at_lo", "ln", "hq_ok", "c1_ok", "u_ok", "um_step", "us_ok", "c2_ok", "base_ok", "o_ok"))
        xb_ok, pow_ok, uround_ok = (sem(n) for n in ("xb_ok", "pow_ok", "uround_ok"))
        LN_STEPS = 13

        w_gv_rows = a["L0_ffn_w_gv"].rearrange("(n m p) i -> n p m i", m=4, p=P)
        w_out_rows = a["L0_ffn_w_out"].rearrange("(n p) i -> n p i", p=P)

        def bf(b):
            return bank[b][:].bitcast(BF16)

        def iterations(eng, emit):
            loop_to = UN + (NTILE - UN) // UN * UN
            for i in range(UN):
                emit(i, i)
            with eng.Fori(1, loop_to // UN) as k:
                for m in range(UN):
                    emit(k * UN + m, m)
            for i in range(loop_to, NTILE + 3):
                emit(i, i % UN)

        def active(i, lag):
            return not isinstance(i, int) or 0 <= i - lag < NTILE

        def weight_block(eng, c, w):
            src = bf(W_BANKS[(2 * c + w) % 4])
            if c < GVC:
                src = src.rearrange("p (m k o) -> p m k o", m=2, k=KC)
                at = (4 * c + 2 * w) * P
                dst = wgvT[:, :, at:at + 2 * P].rearrange("p k (m o) -> p m k o", m=2)
            else:
                src = src.rearrange("p (k o) -> p k o", k=8)
                dst = woutT[:, 8 * w:8 * w + 8, (c - GVC) * P:(c - GVC + 1) * P]
            if w == 1:
                return nc.scalar.activation(dst, src, ACT.Copy)
            return nc.vector.tensor_copy(dst, src)

        with nc.Block() as block:
            @block.sync
            def _(sp):
                for n in range(2 * NCH):
                    c = n % NCH
                    if n >= 3:
                        if n - 3 < NCH:
                            sp.wait_ge(asum_ok, n - 2)
                        else:
                            sp.wait_ge(tern_step, 3 * (n - 3 - NCH) + 1)
                    dst = stage[:, n % 3, :]
                    if c < GVC:
                        sp.dma_start(dst.rearrange("p (m i) -> p m i", m=4), w_gv_rows[c]).then_inc(w_ld[n % 3], 16)
                    else:
                        sp.dma_start(dst, w_out_rows[c - GVC]).then_inc(w_ld[n % 3], 16)

                def emit(i, m):
                    if active(i, 0):
                        if not (isinstance(i, int) and i < 2):
                            sp.wait_ge(at_t, i - 1)
                            sp.wait_ge(xb_ok, i - 1)
                        sp.dma_start(attn_in[:, m % 2, :], attn_dram[bass.ds(i * P, P), :]).then_inc(tile_ld[m % 2], 16)
                        sp.dma_start(x_in[:, m % 2, :], x_rows[bass.ds(i * P, P), :]).then_inc(tile_ld[m % 2], 16)
                    if active(i, 3):
                        t = i - 3
                        sp.wait_ge(o_ok, t + 1)
                        sp.dma_start(out_rows[bass.ds(t * P, P), :], o_sb[:, (m - 3) % 2, :]).then_inc(out_st[(m - 3) % 2], 16)

                iterations(sp, emit)
                for p in range(2):
                    sp.wait_ge(out_st[p], 16 * ((NTILE + 1 - p) // 2))

            @block.gpsimd
            def _(pool):
                pool.memset(identf[:], 1.0).then_inc(ident_ok, 1)
                pool.wait_ge(ident_ok, 1)
                pool.affine_select(out=identf[:], in_=identf[:], compare_op=ALU.is_equal, fill=0.0, base=0,
                                   pattern=[[-1, P]], channel_multiplier=1).then_inc(ident_ok, 1)
                pool.wait_ge(ident_ok, 2)
                pool.tensor_copy(identb[:], identf[:]).then_inc(ident_ok, 1)
                pool.memset(ones[:], 1.0).then_inc(const_ok, 1)
                pool.memset(minus_half[:], -0.5).then_inc(const_ok, 1)
                pool.wait_ge(const_ok, 2)

                def emit(i, m):
                    if active(i, 0):
                        pool.wait_ge(tile_ld[m % 2], ((i - m) // 2 + m // 2 + 1) * 32 if isinstance(i, int)
                                     else (i - m) * 16 + (m // 2 + 1) * 32)
                        if isinstance(i, int) and i == 0:
                            pool.wait_ge(bo_ok, 1)
                        else:
                            pool.wait_ge(ln, (i - 1) * LN_STEPS + 1)
                    if active(i, 2):
                        t = i - 2
                        pool.wait_ge(us_ok, t + 1)
                        if not (isinstance(i, int) and i == 2):
                            pool.wait_ge(uq_ok, t)
                    if active(i, 0):
                        pool.tensor_tensor(xb[:], x_in[:, m % 2, :], bo_bc[:], ALU.add).then_inc(xb_ok, 1)
                    if active(i, 2):
                        pool.tensor_scalar(uround[:], u[:], us[:, 3:4], ROUND, ALU.mult, ALU.add).then_inc(uround_ok, 1)
                    if active(i, 0):
                        pool.wait_ge(ln, i * LN_STEPS + 4)
                        pool.tensor_tensor(rs[:, 0, 1:2], rs[:, 0, 0:1], minus_half[:], ALU.pow).then_inc(pow_ok, 1)
                        pool.wait_ge(ln, i * LN_STEPS + 6)
                        pool.tensor_tensor(rs[:, 1, 1:2], rs[:, 1, 0:1], minus_half[:], ALU.pow).then_inc(pow_ok, 1)

                iterations(pool, emit)

            @block.scalar
            def _(act):
                act.dma_start(gates[:, 0:1], a["g_xattn"].partition_broadcast(P)).then_inc(small_ld, 16)
                act.dma_start(gates[:, 1:2], a["g_ffn"].partition_broadcast(P)).then_inc(small_ld, 16)
                act.dma_start(bo_bc[:], a["L0_xattn_bo"].partition_broadcast(P)).then_inc(small_ld, 16)
                act.dma_start(wn_bc[:], a["L0_ffn_w_norm"].partition_broadcast(P)).then_inc(small_ld, 16)
                act.dma_start(u[:].rearrange("p (m i) -> p m i", m=KC),
                              a["L0_xattn_Wo"].rearrange("(m p) i -> p m i", p=P)).then_inc(wo_ld, 16)
                act.wait_ge(small_ld, 64)
                nc.scalar.activation(gates[:, 2:4], gates[:, 0:2], ACT.Tanh).then_inc(tanh_ok, 1)
                for m in range(KC):
                    act.wait_ge(wo_t, m + 1)
                    nc.scalar.activation(woT[0][:, :, m * P:(m + 1) * P], bank[(AT, WO)[m % 2]][:].rearrange(
                        "p (c o) -> p c o", c=KC), ACT.Copy).then_inc(wo_hi, 1)
                for c in range(NCH):
                    act.wait_ge(tern_step, 3 * c + 2)
                    if c >= 2:
                        act.wait_ge(w_t, 2 * (c - 1))
                    nc.scalar.activation(ternb[:, c % 2, :], tern[:, c % 2, :], ACT.Copy, bias=-ROUND).then_inc(ternb_ok, 1)
                    act.wait_ge(w_t, 2 * c + 2)
                    weight_block(act, c, 1).then_inc(w_ok1, 1)

                def emit(i, m):
                    if active(i, 0):
                        act.wait_ge(at_t, i + 1)
                        if not (isinstance(i, int) and i == 0):
                            act.wait_ge(wo_mm, i)
                        nc.scalar.activation(aT[0][:], bank[AT][:].rearrange("p (c t) -> p c t", c=KC), ACT.Copy
                                             ).then_inc(at_hi, 1)
                    if active(i, 1):
                        act.wait_ge(h_t, i)
                        nc.scalar.activation(hT[:], bf(QT)[:, 0:KC * P].rearrange("p (c t) -> p c t", c=KC), ACT.Copy
                                             ).then_inc(hT_ok, 1)
                    if active(i, 2):
                        t = i - 2
                        act.wait_ge(uround_ok, t + 1)
                        if not (isinstance(i, int) and i == 2):
                            act.wait_ge(u_t, 2 * t)
                        nc.scalar.activation(uq[:], uround[:], ACT.Copy, bias=-ROUND).then_inc(uq_ok, 1)

                    def silu(j):
                        t = i - 1
                        act.wait_ge(gv_mm, t * JB + j + 1)
                        if j == 0:
                            act.wait_ge(c1_ok, t + 1)
                        if not (isinstance(i, int) and i == 1 and j < 2):
                            act.wait_ge(u_ok, t * JB + j - 1)
                        nc.scalar.activation(sg[:, j % 2, :], bank[GV[j % 2][1]][:], ACT.Silu,
                                             scale=c1[:, (m - 1) % UN:(m - 1) % UN + 1]).then_inc(sg_ok, 1)

                    if active(i, 1):
                        silu(0)
                    if active(i, 0):
                        act.wait_ge(ln, i * LN_STEPS + 5)
                        nc.scalar.activation(hround[:], y[:], ACT.Square, accum_out=rs[:, 1, 2:3]).then_inc(sq_ok, 1)
                    if active(i, 1):
                        silu(1)
                    if active(i, 2):
                        t = i - 2
                        if not (isinstance(i, int) and i == 2):
                            act.wait_ge(out_mm, t)
                        for w, b in enumerate((QT, AT)):
                            act.wait_ge(u_t, 2 * t + w + 1)
                            nc.scalar.activation(uT[:, 8 * w:8 * w + 8, :], bf(b).rearrange("p (c t) -> p c t", c=8), ACT.Copy
                                                 ).then_inc(uT_ok, 1)
                    if active(i, 1):
                        silu(2)
                        silu(3)

                iterations(act, emit)

            @block.vector
            def _(dve):
                for m in range(KC):
                    dve.wait_ge(wo_hi, m + 1)
                    hi, lo = (t[:, :, m * P:(m + 1) * P] for t in woT)
                    nc.vector.tensor_tensor(lo, bank[(AT, WO)[m % 2]][:].rearrange("p (c o) -> p c o", c=KC),
                                            hi.bitcast(F32), ALU.subtract).then_inc(wo_lo, 1)
                for c in range(NCH):
                    dve.wait_ge(w_ld[c % 3], 16 * (c // 3 + 1))
                    nc.vector.tensor_reduce(abs_sum[:, c:c + 1], stage[:, c % 3, :], AX_X, ALU.add,
                                            apply_absolute_value=True).then_inc(asum_ok, 1)
                dve.wait_ge(wsum_mm, 1)
                nc.vector.tensor_reduce(wstat[:, 0, 0:1], bank[OUT][:, 0:GVC], AX_X, ALU.add).then_inc(wstat_step, 1)
                nc.vector.tensor_reduce(wstat[:, 1, 0:1], bank[OUT][:, GVC:NCH], AX_X, ALU.add).then_inc(wstat_step, 1)
                dve.wait_ge(wstat_step, 2)
                for n, count in enumerate((2 * HID * H, HID * H)):
                    nc.vector.tensor_scalar(wstat[:, n, 1:2], wstat[:, n, 0:1], 1.0 / count, EPS, ALU.mult, ALU.max
                                            ).then_inc(wstat_step, 1)
                dve.wait_ge(wstat_step, 4)
                for n in range(2):
                    nc.vector.reciprocal(wstat[:, n, 2:3], wstat[:, n, 1:2]).then_inc(wstat_step, 1)
                    nc.vector.tensor_scalar(wstat[:, n, 3:4], wstat[:, n, 1:2], 1.0 / QB, None, ALU.mult).then_inc(wstat_step, 1)
                dve.wait_ge(wstat_step, 8)
                dve.wait_ge(tanh_ok, 1)
                nc.vector.tensor_scalar(wstat[:, 1, 3:4], wstat[:, 1, 3:4], gates[:, 3:4], None, ALU.mult).then_inc(wstat_step, 1)
                nc.vector.tensor_scalar(bo_bc[:], bo_bc[:], gates[:, 2:3], None, ALU.mult).then_inc(bo_ok, 1)

                def way_back(c):
                    dve.wait_ge(w_t, 2 * c + 1)
                    weight_block(dve, c, 0).then_inc(w_ok0, 1)

                for c in range(NCH):
                    n = NCH + c
                    dve.wait_ge(w_ld[n % 3], 16 * (n // 3 + 1))
                    if c >= 2:
                        dve.wait_ge(ternb_ok, c - 1)
                    buf = stage[:, n % 3, :]
                    s = wstat[:, 0 if c < GVC else 1, 2:3]
                    nc.vector.tensor_scalar(tern[:, c % 2, :], buf, s, ROUND, ALU.mult, ALU.add).then_inc(tern_step, 1)
                    dve.wait_ge(tern_step, 3 * c + 1)
                    nc.vector.tensor_scalar(tern[:, c % 2, :], tern[:, c % 2, :], ROUND - 1.0, ROUND + 1.0, ALU.max, ALU.min
                                            ).then_inc(tern_step, 2)
                    if c >= 1:
                        way_back(c - 1)
                way_back(NCH - 1)

                def carrier():
                    nc.vector.tensor_copy(carried[:, 1:2], ones[:, 0:1])

                def emit(i, m):
                    def products(j):
                        t = i - 1
                        dve.wait_ge(sg_ok, t * JB + j + 1)
                        if not (isinstance(i, int) and i == 1) and j == 0:
                            dve.wait_ge(uround_ok, t)
                        cols = slice(j * 512, (j + 1) * 512)
                        nc.vector.scalar_tensor_tensor(u[:, cols], bank[GV[j % 2][0]][:], c1[:, (m - 1) % UN:(m - 1) % UN + 1],
                                                       sg[:, j % 2, :], ALU.mult, ALU.mult).then_inc(u_ok, 1)
                        dve.wait_ge(u_ok, t * JB + j + 1)
                        nc.vector.tensor_reduce(um[:, j:j + 1], u[:, cols], AX_X, ALU.max, apply_absolute_value=True
                                                ).then_inc(um_step, 1)

                    step = [0]

                    def link(ins, wait=True):
                        step[0] += 1
                        ins.then_inc(ln, 1)
                        if wait:
                            dve.wait_ge(ln, i * LN_STEPS + step[0])

                    if active(i, 0):
                        dve.wait_ge(at_hi, i + 1)
                        nc.vector.tensor_tensor(aT[1][:], bank[AT][:].rearrange("p (c t) -> p c t", c=KC),
                                                aT[0][:].bitcast(F32), ALU.subtract).then_inc(at_lo, 1)
                    if active(i, 3):
                        t = i - 3
                        dve.wait_ge(out_mm, t + 1)
                        if not (isinstance(i, int) and i < 5):
                            dve.wait_ge(out_st[(m - 3) % 2], ((t - (t % 2)) // 2) * 16 if isinstance(i, int)
                                        else (i - m) * 8 + ((m - 3) // 2) * 16)
                        nc.vector.scalar_tensor_tensor(o_sb[:, (m - 3) % 2, :], bank[OUT][:], c2[:, (m - 3) % UN:(m - 3) % UN + 1],
                                                       base[:, (m - 3) % UN, :], ALU.mult, ALU.add).then_inc(o_ok, 1)
                    if active(i, 0):
                        dve.wait_ge(wo_mm, i + 1)
                        dve.wait_ge(xb_ok, i + 1)
                        link(nc.vector.scalar_tensor_tensor(x1[:], bank[WO][:], gates[:, 2:3], xb[:], ALU.mult, ALU.add))
                        link(nc.vector.bn_stats(bn[:], x1[:]))
                        carrier()
                        link(nc.vector.bn_aggr(mv[:], bn[:]))
                        link(nc.vector.tensor_scalar(rs[:, 0, 0:1], mv[:, 1:2], EPS, None, ALU.add), False)
                        dve.wait_ge(pow_ok, 2 * i + 1)
                        link(nc.vector.tensor_scalar(y[:], x1[:], mv[:, 0:1], rs[:, 0, 1:2], ALU.subtract, ALU.mult), False)
                    if active(i, 1):
                        products(0)
                    if active(i, 0):
                        dve.wait_ge(sq_ok, i + 1)
                        link(nc.vector.tensor_scalar(rs[:, 1, 0:1], rs[:, 1, 2:3], 1.0 / H, EPS, ALU.mult, ALU.add), False)
                        nc.vector.scalar_tensor_tensor(base[:, m % UN, :], y[:], gates[:, 3:4], x1[:], ALU.mult, ALU.add
                                                       ).then_inc(base_ok, 1)
                        dve.wait_ge(pow_ok, 2 * i + 2)
                        link(nc.vector.scalar_tensor_tensor(h[:], y[:], rs[:, 1, 1:2], wn_bc[:], ALU.mult, ALU.mult))
                        link(nc.vector.tensor_reduce(hs[:, 0:1], h[:], AX_X, ALU.max, apply_absolute_value=True))
                        link(nc.vector.tensor_scalar(hs[:, 1:2], hs[:, 0:1], EPS, None, ALU.max))
                        link(nc.vector.reciprocal(hs[:, 2:3], hs[:, 1:2]))
                        nc.vector.tensor_scalar(c1[:, m % UN:m % UN + 1], hs[:, 1:2], wstat[:, 0, 3:4], None, ALU.mult
                                                ).then_inc(c1_ok, 1)
                        link(nc.vector.tensor_scalar(hs[:, 3:4], hs[:, 2:3], QB, None, ALU.mult))
                        link(nc.vector.tensor_scalar(hround[:], h[:], hs[:, 3:4], ROUND, ALU.mult, ALU.add))
                        if not (isinstance(i, int) and i == 0):
                            dve.wait_ge(h_t, i)
                        link(nc.vector.tensor_scalar(hq[:], hround[:], ROUND, None, ALU.subtract), False)
                    if active(i, 1):
                        t = i - 1
                        for j in range(1, JB):
                            products(j)
                        if not (isinstance(i, int) and i == 1):
                            dve.wait_ge(uround_ok, t)
                        dve.wait_ge(um_step, t * (JB + 3) + JB)
                        nc.vector.tensor_reduce(us[:, 0:1], um[:], AX_X, ALU.max).then_inc(um_step, 1)
                        dve.wait_ge(um_step, t * (JB + 3) + JB + 1)
                        nc.vector.tensor_scalar(us[:, 1:2], us[:, 0:1], EPS, None, ALU.max).then_inc(um_step, 1)
                        dve.wait_ge(um_step, t * (JB + 3) + JB + 2)
                        nc.vector.reciprocal(us[:, 2:3], us[:, 1:2]).then_inc(um_step, 1)
                        dve.wait_ge(um_step, t * (JB + 3) + JB + 3)
                        nc.vector.tensor_scalar(us[:, 3:4], us[:, 2:3], QB, None, ALU.mult).then_inc(us_ok, 1)
                        nc.vector.tensor_scalar(c2[:, (m - 1) % UN:(m - 1) % UN + 1], us[:, 1:2], wstat[:, 1, 3:4], None, ALU.mult
                                                ).then_inc(c2_ok, 1)

                dve.wait_ge(wstat_step, 9)
                dve.wait_ge(const_ok, 2)
                iterations(dve, emit)

            @block.tensor
            def _(pe):
                pe.wait_ge(ident_ok, 3)
                pe.wait_ge(wo_ld, 16)
                for m in range(KC):
                    if m >= 2:
                        pe.wait_ge(wo_lo, m - 1)
                    for c in range(KC):
                        last = nc.tensor.transpose(bank[(AT, WO)[m % 2]][:, c * P:(c + 1) * P],
                                                   u[:, m * H + c * P:m * H + (c + 1) * P], identf[:])
                    last.then_inc(wo_t, 1)
                pe.wait_ge(const_ok, 2)
                pe.wait_ge(asum_ok, NCH)
                nc.tensor.matmul(bank[OUT][:, 0:NCH], ones[:], abs_sum[:], start=True, stop=True).then_inc(wsum_mm, 1)
                for c in range(NCH):
                    pe.wait_ge(ternb_ok, c + 1)
                    for w in range(2):
                        if c >= 2:
                            pe.wait_ge((w_ok0, w_ok1)[w], c - 1)
                        dst = bf(W_BANKS[(2 * c + w) % 4])
                        for k in range(8):
                            at = (2 * w * KC + k) * P if c < GVC else (8 * w + k) * P
                            last = nc.tensor.transpose(dst[:, k * P:(k + 1) * P], ternb[:, c % 2, at:at + P], identb[:])
                        last.then_inc(w_t, 1)
                pe.wait_ge(w_ok0, NCH)
                pe.wait_ge(w_ok1, NCH)
                pe.wait_ge(wo_lo, KC)

                def emit(i, m):
                    if active(i, 0):
                        pe.wait_ge(tile_ld[m % 2], ((i - m) // 2 + m // 2 + 1) * 32 if isinstance(i, int)
                                   else (i - m) * 16 + (m // 2 + 1) * 32)
                        if not (isinstance(i, int) and i < 3):
                            pe.wait_ge(uT_ok, 2 * (i - 2))
                        for c in range(KC):
                            last = nc.tensor.transpose(bank[AT][:, c * P:(c + 1) * P], attn_in[:, m % 2, c * P:(c + 1) * P], identf[:])
                        last.then_inc(at_t, 1)
                    if active(i, 3):
                        t = i - 3
                        pe.wait_ge(uT_ok, 2 * t + 2)
                        if not (isinstance(i, int) and i == 3):
                            pe.wait_ge(o_ok, t)
                        for k in range(HC):
                            last = nc.tensor.matmul(bank[OUT][:], uT[:, k, :], woutT[:, k, :], start=(k == 0), stop=(k == HC - 1))
                        last.then_inc(out_mm, 1)
                    if active(i, 1):
                        pe.wait_ge(ln, i * LN_STEPS)
                        for c in range(KC):
                            last = nc.tensor.transpose(bf(QT)[:, c * P:(c + 1) * P], hq[:, c * P:(c + 1) * P], identb[:])
                        last.then_inc(h_t, 1)
                    if active(i, 0):
                        pe.wait_ge(at_lo, i + 1)
                        if not (isinstance(i, int) and i == 0):
                            pe.wait_ge(ln, (i - 1) * LN_STEPS + 1)
                        for c in range(KC):
                            nc.tensor.matmul(bank[WO][:], aT[0][:, c, :], woT[0][:, c, :], start=(c == 0), stop=False)
                            nc.tensor.matmul(bank[WO][:], aT[0][:, c, :], woT[1][:, c, :], start=False, stop=False)
                            last = nc.tensor.matmul(bank[WO][:], aT[1][:, c, :], woT[0][:, c, :], start=False, stop=(c == KC - 1))
                        last.then_inc(wo_mm, 1)

                    def gate_value(j):
                        t = i - 1
                        if not (isinstance(i, int) and i == 1 and j < 2):
                            pe.wait_ge(u_ok, t * JB + j - 1)
                        for w in range(2):
                            for c in range(KC):
                                last = nc.tensor.matmul(bank[GV[j % 2][w]][:], hT[:, c, :],
                                                        wgvT[:, c, w * HID + j * 512:w * HID + (j + 1) * 512],
                                                        start=(c == 0), stop=(c == KC - 1))
                        last.then_inc(gv_mm, 1)

                    if active(i, 1):
                        pe.wait_ge(hT_ok, i)
                        gate_value(0)
                        gate_value(1)
                    if active(i, 2):
                        t = i - 2
                        pe.wait_ge(uq_ok, t + 1)
                        if active(i, 1):
                            pe.wait_ge(hT_ok, i)
                        if active(i, 0):
                            pe.wait_ge(at_lo, i + 1)
                        for w, b in enumerate((QT, AT)):
                            for k in range(8):
                                last = nc.tensor.transpose(bf(b)[:, k * P:(k + 1) * P], uq[:, (8 * w + k) * P:(8 * w + k + 1) * P],
                                                           identb[:])
                            last.then_inc(u_t, 1)
                    if active(i, 1):
                        gate_value(2)
                        gate_value(3)

                iterations(pe, emit)


_INS = ["x", "ctx_2048", "mask_BxS2_ff1", "g_xattn", "g_ffn", "L0_xattn_Wq", "L0_xattn_bq", "L0_xattn_Wk", "L0_xattn_bk",
        "L0_xattn_Wv", "L0_xattn_bv", "L0_xattn_Wqf", "L0_xattn_Wkf", "L0_xattn_Wo", "L0_xattn_bo", "L0_ffn_w_norm",
        "L0_ffn_w_gv", "L0_ffn_w_out"]


def kernel(**inputs):
    import numpy as _np
    import concourse.bacc as _bacc
    from concourse import mybir as _mybir
    from concourse.bass_utils import run_bass_kernel_spmd as _run

    nc = _bacc.Bacc("TRN2", target_bir_lowering=False, num_devices=1)
    arrays, args = {}, {}
    for name in _INS:
        arr = _np.ascontiguousarray(inputs[name])
        arrays[f"in_{name}"] = arr
        args[name] = nc.dram_tensor(f"in_{name}", arr.shape, _mybir.dt.from_np(arr.dtype), kind="ExternalInput").ap()
    out = nc.dram_tensor("out_dram", inputs["x"].shape, _mybir.dt.float32, kind="ExternalOutput").ap()
    flamingo_gated_layer(nc, args, out)
    r = _run(nc, [arrays], core_ids=[0])
    return r.results[0]["out_dram"]
```
